# Optimizing a Trainium2 kernel written in Bass

```python
import numpy as np
import jax
import jax.numpy as jnp

def _softmax(x, axis=-1):
    return jax.nn.softmax(x, axis=axis)

def _gelu(x):
    return jax.nn.gelu(x, approximate=True)

def _silu(x):
    return jax.nn.silu(x)

def _sigmoid(x):
    return jax.nn.sigmoid(x)

def _layernorm(x, axis=-1, eps=1e-05):
    m = jnp.mean(x, axis=axis, keepdims=True)
    v = jnp.var(x, axis=axis, keepdims=True)
    return (x - m) / jnp.sqrt(v + eps)

def _scatter_add(tgt, idx, src, axis=0):
    return tgt.at[idx].add(src)

def _segment_sum(src, seg, n):
    return jax.ops.segment_sum(src, seg, n)
kernel_name = 'mk_xattn_seq_d1_seqx_r2_31fe16'

def setup_inputs(seed: int=0):
    np.random.seed(seed)
    _w = jnp.asarray

    def _rec_inputs():
        import jax
        import jax.numpy as jnp
        _rk = jax.random.key(seed)
        x = -0.000125 + 0.9999 * jax.random.normal(jax.random.fold_in(_rk, 1), (16, 256, 512), jnp.float32)
        _lenS = 256 - jax.random.randint(jax.random.fold_in(_rk, 7), (16,), 0, max(1, 256 // 4) + 1, jnp.int32)
        _lenS2 = 256 - jax.random.randint(jax.random.fold_in(_rk, 8), (16,), 0, max(1, 256 // 4) + 1, jnp.int32)
        _ctx_1024P = jax.random.normal(jax.random.fold_in(_rk, 11), (16, 16, 512), jnp.float32)
        _ctx_1024c = jax.random.dirichlet(jax.random.fold_in(_rk, 511), 0.3 * jnp.ones((16,), jnp.float32), (16, 256))
        _ctx_1024t = jnp.einsum('bsk,bkd->bsd', _ctx_1024c, _ctx_1024P)
        _ctx_1024t = _ctx_1024t * jax.lax.rsqrt(jnp.mean(jnp.square(_ctx_1024t)) + 1e-12) * 0.953939
        ctx_1024 = -1.52775e-05 + 0.999936 * (_ctx_1024t + 0.3 * jax.random.normal(jax.random.fold_in(_rk, 611), (16, 256, 512), jnp.float32))
        return (x, ctx_1024)
    x, ctx_1024 = _rec_inputs()

    def _L0_xattn_setup():
        import jax, jax.numpy as jnp
        import numpy as np
        EMB = 512
        key = jax.random.key(seed)
        ks = jax.random.split(key, 8)
        B, Lq, Lk, D = (16, 1024, 1024, EMB)
        scale = 1.0 / np.sqrt(D)
        return {'text_embeds': jax.random.normal(ks[0], (B, Lq, D), jnp.float32), 'step_embeds': jax.random.normal(ks[1], (B, Lk, D), jnp.float32), 'Wq': jax.random.normal(ks[2], (D, D), jnp.float32) * scale, 'bq': jnp.zeros((D,), jnp.float32), 'Wk': jax.random.normal(ks[3], (D, D), jnp.float32) * scale, 'bk': jnp.zeros((D,), jnp.float32), 'Wv': jax.random.normal(ks[4], (D, D), jnp.float32) * scale, 'bv': jnp.zeros((D,), jnp.float32)}
    _L0_xattn_all = _L0_xattn_setup()
    _L0_xattn_in = {k: v for k, v in _L0_xattn_all.items() if k in ('Wq', 'bq', 'Wk', 'bk', 'Wv', 'bv')}
    del _L0_xattn_all
    return {'x': x, 'ctx_1024': ctx_1024, 'L0_xattn_Wq': _L0_xattn_in['Wq'], 'L0_xattn_bq': _L0_xattn_in['bq'], 'L0_xattn_Wk': _L0_xattn_in['Wk'], 'L0_xattn_bk': _L0_xattn_in['bk'], 'L0_xattn_Wv': _L0_xattn_in['Wv'], 'L0_xattn_bv': _L0_xattn_in['bv']}

def reference(x, ctx_1024, L0_xattn_Wq, L0_xattn_bq, L0_xattn_Wk, L0_xattn_bk, L0_xattn_Wv, L0_xattn_bv):
    import jax
    import jax.numpy as jnp

    def _L0_xattn_ref(text_embeds, step_embeds, Wq, bq, Wk, bk, Wv, bv):
        import jax, jax.numpy as jnp
        import numpy as np
        EMB = 512
        Q = jnp.einsum('bqd,de->bqe', text_embeds, Wq) + bq
        K = jnp.einsum('bkd,de->bke', step_embeds, Wk) + bk
        V = jnp.einsum('bkd,de->bke', step_embeds, Wv) + bv
        scores = jnp.einsum('bqe,bke->bqk', Q, K)
        attn = jax.nn.softmax(scores, axis=-1)
        out = jnp.einsum('bqk,bke->bqe', attn, V)
        return out + text_embeds
    x = _L0_xattn_ref(x, ctx_1024, L0_xattn_Wq, L0_xattn_bq, L0_xattn_Wk, L0_xattn_bk, L0_xattn_Wv, L0_xattn_bv)
    return x

_drawn_inputs = setup_inputs


def setup_inputs(seed=0):
    import zlib

    import numpy as np

    out = dict(_drawn_inputs(seed))
    spreads = {'L0_xattn_bq': (0.0, 0.1), 'L0_xattn_bk': (0.0, 0.1), 'L0_xattn_bv': (0.0, 0.1)}
    factors = {}
    for name, (base, spread) in spreads.items():
        noise = np.random.default_rng([zlib.crc32(name.encode()), seed]).standard_normal(out[name].shape)
        drawn = base * np.exp(spread * noise) if base else spread * noise
        out[name] = jnp.asarray(drawn.astype(out[name].dtype))
    for name, factor in factors.items():
        out[name] = (out[name] * factor).astype(out[name].dtype)
    return out
```

```python
from contextlib import ExitStack

import concourse.bass as bass
from concourse import mybir

F32 = mybir.dt.float32
F32R = mybir.dt.float32r
ALU = mybir.AluOpType
ACT = mybir.ActivationFunctionType
AX_X = mybir.AxisListType.X

P = 128
PB = 2


def xattn_program(nc, x, xT, cT, WqT, WkT, Wv, bq, bk, bv, out):
    B, L, D = x.shape
    PAIRS = B // PB
    DC = D // P
    LT = L // P
    COLS = PB * L
    TILES = PB * LT
    assert COLS == 512 and D == 512 and DC == TILES == 4 and LT == 2

    with ExitStack() as ctx:
        def sb(name, shape, dt=F32):
            return ctx.enter_context(nc.sbuf_tensor(name, shape, dt))

        def sem(name):
            return ctx.enter_context(nc.semaphore(name))

        wk_raw = sb("wk_raw", [P, DC, D])
        wk_hi, wk_lo = sb("wk_hi", [P, DC, D], F32R), sb("wk_lo", [P, DC, D], F32R)
        wv_hi, wv_lo = sb("wv_hi", [P, DC, D], F32R), sb("wv_lo", [P, DC, D], F32R)
        m_hi, m_lo = sb("m_hi", [P, DC, D], F32R), sb("m_lo", [P, DC, D], F32R)
        x_raw = sb("x_raw", [P, DC, COLS])
        x_hi, x_lo = sb("x_hi", [P, DC, COLS], F32R), sb("x_lo", [P, DC, COLS], F32R)
        c_raw = sb("c_raw", [P, DC, COLS])
        c_hi, c_lo = sb("c_hi", [P, DC, COLS], F32R), sb("c_lo", [P, DC, COLS], F32R)
        t_hi, t_lo = sb("t_hi", [P, DC, COLS], F32R), sb("t_lo", [P, DC, COLS], F32R)
        v_hi, v_lo = sb("v_hi", [P, TILES, D], F32R), sb("v_lo", [P, TILES, D], F32R)
        probs = sb("probs", [P, PB, LT, L])
        pT_hi, pT_lo = sb("pT_hi", [P, PB, LT, L], F32R), sb("pT_lo", [P, PB, LT, L], F32R)
        x_rows = sb("x_rows", [P, TILES, D])
        x_bv = sb("x_bv", [P, TILES, D])
        out_rows = sb("out_rows", [P, TILES, D])
        bv_rows = sb("bv_rows", [P, D])
        u_rows = sb("u_rows", [P, D])
        u_parts = sb("u_parts", [P, D])
        tv_parts = sb("tv_parts", [P, D])
        scaled = sb("scaled", [P, 2, D])
        unused = sb("unused", [P, D])
        bq_col, bk_col = sb("bq_col", [P, DC]), sb("bk_col", [P, DC])
        bqbk = sb("bqbk", [P, DC])
        tbias = sb("tbias", [P, DC])
        r0 = sb("r0", [P, 1])
        r_rows = sb("r_rows", [P, TILES])
        negmax = sb("negmax", [P, TILES])
        exp_bias = sb("exp_bias", [P, TILES])
        rowsum = sb("rowsum", [P, TILES])
        inv_sum = sb("inv_sum", [P, TILES])
        ident = sb("ident", [P, P])
        ones = sb("ones", [P, P])
        wq_raw, wv_raw = x_bv, out_rows
        wq_hi, wq_lo = v_hi, v_lo

        main = [ctx.enter_context(nc.psum_tensor(f"main{k}", [P, 512], F32)) for k in range(4)]
        score = [ctx.enter_context(nc.psum_tensor(f"score{b}", [P, LT, L], F32)) for b in range(PB)]
        probT = [ctx.enter_context(nc.psum_tensor(f"probT{b}", [P, LT, L], F32)) for b in range(PB)]
        m_bank = [score[0], score[1], probT[0], probT[1]]

        wk_loaded = [sem(f"wk_loaded{c}") for c in range(DC)]
        wq_loaded = [sem(f"wq_loaded{c}") for c in range(DC)]
        wv_loaded, bqk_loaded, bv_loaded = sem("wv_loaded"), sem("bqk_loaded"), sem("bv_loaded")
        x_loaded, c_loaded, rows_loaded, stored = sem("x_loaded"), sem("c_loaded"), sem("rows_loaded"), sem("stored")
        wk_hi_done, wq_hi_done, wv_hi_done, m_hi_done = sem("wk_hi_done"), sem("wq_hi_done"), sem("wv_hi_done"), sem("m_hi_done")
        wk_lo_done, wq_lo_done, wv_lo_done, m_lo_done = sem("wk_lo_done"), sem("wq_lo_done"), sem("wv_lo_done"), sem("m_lo_done")
        x_hi_done, c_hi_done, t_hi_done, v_hi_done, pT_hi_done = (
            sem("x_hi_done"), sem("c_hi_done"), sem("t_hi_done"), sem("v_hi_done"), sem("pT_hi_done"))
        x_lo_done, c_lo_done, pT_lo_done = sem("x_lo_done"), sem("c_lo_done"), sem("pT_lo_done")
        main_drained = sem("main_drained")
        m_done, t_done, v_done, s_done, pT_done, o_done = (
            sem("m_done"), sem("t_done"), sem("v_done"), sem("s_done"), sem("pT_done"), sem("o_done"))
        bias_sums, bias_copied = sem("bias_sums"), sem("bias_copied")
        max_done, exp_bias_done, exp_done, inv_done, r_done = (
            sem("max_done"), sem("exp_bias_done"), sem("exp_done"), sem("inv_done"), sem("r_done"))
        ident_zero, consts_done, pool_step, parts_done, x_bv_done = (
            sem("ident_zero"), sem("consts_done"), sem("pool_step"), sem("parts_done"), sem("x_bv_done"))

        def drained_v(j, k):
            return j * 12 + (TILES + k + 1)

        def drained_t_next(j, k):
            return j * 12 + (2 * TILES + k + 1)

        def drained_o(j, k):
            return j * 12 + (3 * TILES + k + 1)

        def rows_of(dram, j):
            return dram[bass.ds(j * PB, PB)].rearrange("b (p t) d -> p b (t d)", t=LT)

        def sb_rows(tensor):
            return tensor[:, :, :].rearrange("p (b t) d -> p b (t d)", b=PB)

        block = ctx.enter_context(nc.Block())

        @block.sync
        def _(sp):
            sp.dma_start(bq_col[:, :], bq).then_inc(bqk_loaded, 16)
            sp.dma_start(bk_col[:, :], bk).then_inc(bqk_loaded, 16)
            for c in range(DC):
                sp.dma_start(wk_raw[:, c, :], WkT[c]).then_inc(wk_loaded[c], 16)
                sp.dma_start(wq_raw[:, c, :], WqT[c]).then_inc(wq_loaded[c], 16)
            sp.dma_start(x_raw[:, :, :], xT[0]).then_inc(x_loaded, 16)
            sp.dma_start(c_raw[:, :, :], cT[0]).then_inc(c_loaded, 16)
            sp.dma_start(wv_raw[:, :, :], Wv.rearrange("(c p) e -> p c e", p=P)).then_inc(wv_loaded, 16)
            sp.dma_start(sb_rows(x_rows), rows_of(x, 0)).then_inc(rows_loaded, 16)
            sp.dma_start(bv_rows[:, :], bv.to_broadcast([P, D])).then_inc(bv_loaded, 16)
            sp.wait_ge(x_lo_done, DC)
            sp.dma_start(x_raw[:, :, :], xT[1]).then_inc(x_loaded, 16)
            sp.wait_ge(c_lo_done, DC)
            sp.dma_start(c_raw[:, :, :], cT[1]).then_inc(c_loaded, 16)
            sp.wait_ge(x_bv_done, TILES)
            sp.wait_ge(r_done, TILES)
            sp.dma_start(sb_rows(x_rows), rows_of(x, 1)).then_inc(rows_loaded, 16)

            def store(b, j, drained):
                sp.wait_ge(main_drained, drained)
                sp.dma_start(rows_of(out, j)[:, b], sb_rows(out_rows)[:, b]).then_inc(stored, 16)

            with sp.Fori(0, PAIRS - 2) as j:
                sp.wait_ge(x_lo_done, j * DC + 2 * DC)
                sp.dma_start(x_raw[:, :, :], xT[bass.ds(j + 2, 1)].rearrange("a p c q -> p (a c) q")).then_inc(x_loaded, 16)
                sp.wait_ge(c_lo_done, j * DC + 2 * DC)
                sp.dma_start(c_raw[:, :, :], cT[bass.ds(j + 2, 1)].rearrange("a p c q -> p (a c) q")).then_inc(c_loaded, 16)
                for b in range(PB):
                    store(b, j, drained_o(j, b * LT + LT - 1))
                sp.wait_ge(x_bv_done, j * TILES + 2 * TILES)
                sp.wait_ge(r_done, j * TILES + 2 * TILES)
                sp.dma_start(sb_rows(x_rows), rows_of(x, j + 2)).then_inc(rows_loaded, 16)
            for b in range(PB):
                store(b, PAIRS - 2, drained_o(PAIRS - 2, b * LT + LT - 1))
            for b in range(PB):
                store(b, PAIRS - 1, drained_t_next(PAIRS - 1, b * LT + LT - 1))
            sp.wait_ge(stored, 16 * B)

        @block.gpsimd
        def _(pool):
            pool.memset(ident[:, :], 0.0).then_inc(ident_zero, 1)
            pool.memset(ones[:, :], 1.0).then_inc(consts_done, 1)
            pool.wait_ge(ident_zero, 1)
            pool.affine_select(out=ident[:, :], in_=ident[:, :], compare_op=ALU.not_equal, fill=1.0, base=0,
                               pattern=[[-1, P]], channel_multiplier=1).then_inc(consts_done, 1)

            pool.wait_ge(bqk_loaded, 32)
            steps = [0]

            def step(ins):
                steps[0] += 1
                ins.then_inc(pool_step, 1)

            def weighted_sum(parts, raw, col, loaded):
                for c in range(DC):
                    pool.wait_ge(loaded[c], 16)
                    if c == 0:
                        step(pool.tensor_scalar(parts[:, :], raw[:, c, :], col[:, c:c + 1], None, ALU.mult))
                    else:
                        step(pool.tensor_scalar(scaled[:, c % 2, :], raw[:, c, :], col[:, c:c + 1], None, ALU.mult))
                        pool.wait_ge(pool_step, steps[0])
                        step(pool.tensor_tensor(parts[:, :], parts[:, :], scaled[:, c % 2, :], ALU.add))
                pool.wait_ge(pool_step, steps[0])

            weighted_sum(tv_parts, wk_raw, bq_col, wk_loaded)
            weighted_sum(u_parts, wq_raw, bk_col, wq_loaded)
            pool.tensor_tensor(bqbk[:, :], bq_col[:, :], bk_col[:, :], ALU.mult).then_inc(parts_done, 1)

            def residual(j):
                pool.wait_ge(rows_loaded, j * 16 + 16)
                for t in range(TILES):
                    pool.tensor_tensor(x_bv[:, t, :], x_rows[:, t, :], bv_rows[:, :], ALU.add).then_inc(x_bv_done, 1)

            pool.wait_ge(bv_loaded, 16)
            pool.wait_ge(wq_lo_done, DC)
            residual(0)
            with pool.Fori(0, PAIRS - 1) as j:
                pool.wait_ge(main_drained, drained_o(j, TILES - 1))
                residual(j + 1)

        @block.scalar
        def _(act):
            def hi_of(hi, raw, done):
                nc.scalar.copy(hi, raw).then_inc(done, 1)

            for c in range(DC):
                act.wait_ge(wk_loaded[c], 16)
                hi_of(wk_hi[:, c, :], wk_raw[:, c, :], wk_hi_done)
                act.wait_ge(wq_loaded[c], 16)
                hi_of(wq_hi[:, c, :], wq_raw[:, c, :], wq_hi_done)
            act.wait_ge(x_loaded, 16)
            for c in range(DC):
                hi_of(x_hi[:, c, :], x_raw[:, c, :], x_hi_done)
            for k in range(DC):
                act.wait_ge(m_done, k + 1)
                hi_of(m_hi[:, k, :], m_bank[k][:], m_hi_done)
            act.wait_ge(c_loaded, 16)
            for c in range(DC):
                hi_of(c_hi[:, c, :], c_raw[:, c, :], c_hi_done)

            def t_hi_of(k):
                nc.scalar.activation(t_hi[:, k, :], main[k][:, :], ACT.Identity,
                                     bias=tbias[:, k:k + 1]).then_inc(t_hi_done, 1)

            act.wait_ge(bias_copied, 1)
            for k in range(DC):
                act.wait_ge(t_done, k + 1)
                t_hi_of(k)
            act.wait_ge(wv_loaded, 16)
            for c in range(DC):
                hi_of(wv_hi[:, c, :], wv_raw[:, c, :], wv_hi_done)

            def exponentials(j, b):
                act.wait_ge(exp_bias_done, j * TILES + (b * LT + LT))
                act.wait_ge(pT_done, j * PB)
                for t in range(LT):
                    n = b * LT + t
                    nc.scalar.activation(probs[:, b, t, :], score[b][:, t, :], ACT.Exp, bias=exp_bias[:, n:n + 1],
                                         accum_out=rowsum[:, n:n + 1]).then_inc(exp_done, 1)

            def values_hi(j, k):
                act.wait_ge(v_done, j * TILES + (k + 1))
                hi_of(v_hi[:, k, :], main[k][:, :], v_hi_done)

            def probs_hi(j, b):
                act.wait_ge(pT_done, j * PB + (b + 1))
                hi_of(pT_hi[:, b, :, :], probT[b][:, :, :], pT_hi_done)

            def softmax_and_values(j):
                exponentials(j, 0)
                exponentials(j, 1)
                values_hi(j, 0)
                values_hi(j, 1)
                probs_hi(j, 0)
                values_hi(j, 2)
                probs_hi(j, 1)
                values_hi(j, 3)

            with act.Fori(0, PAIRS - 1) as j:
                act.wait_ge(x_loaded, j * 16 + 32)
                act.wait_ge(t_done, j * DC + DC)
                for c in range(DC):
                    hi_of(x_hi[:, c, :], x_raw[:, c, :], x_hi_done)
                softmax_and_values(j)
                act.wait_ge(c_loaded, j * 16 + 32)
                for k in range(DC):
                    hi_of(c_hi[:, k, :], c_raw[:, k, :], c_hi_done)
                    act.wait_ge(t_done, j * DC + (DC + k + 1))
                    t_hi_of(k)
            softmax_and_values(PAIRS - 1)

        @block.vector
        def _(dve):
            def lo_of(lo, raw, hi, done):
                nc.vector.tensor_tensor(lo, raw, hi.bitcast(F32), ALU.subtract).then_inc(done, 1)

            for c in range(DC):
                dve.wait_ge(wk_hi_done, c + 1)
                lo_of(wk_lo[:, c, :], wk_raw[:, c, :], wk_hi[:, c, :], wk_lo_done)
                dve.wait_ge(wq_hi_done, c + 1)
                lo_of(wq_lo[:, c, :], wq_raw[:, c, :], wq_hi[:, c, :], wq_lo_done)
            for c in range(DC):
                dve.wait_ge(x_hi_done, c + 1)
                lo_of(x_lo[:, c, :], x_raw[:, c, :], x_hi[:, c, :], x_lo_done)
            for k in range(DC):
                dve.wait_ge(m_hi_done, k + 1)
                lo_of(m_lo[:, k, :], m_bank[k][:], m_hi[:, k, :], m_lo_done)
            dve.wait_ge(bias_sums, 1)
            nc.vector.tensor_copy(tbias[:, :], score[1][:, 0, 0:DC]).then_inc(bias_copied, 1)
            nc.vector.reduce_sum(r0[:, :], score[1][:, 0, DC:2 * DC], AX_X).then_inc(bias_copied, 1)
            nc.vector.tensor_copy(u_rows[:, :].rearrange("p (a b) -> p a b", a=LT), score[0][:, :, :]).then_inc(bias_copied, 1)
            for c in range(DC):
                dve.wait_ge(c_hi_done, c + 1)
                lo_of(c_lo[:, c, :], c_raw[:, c, :], c_hi[:, c, :], c_lo_done)

            def t_lo_of(k):
                nc.vector.scalar_tensor_tensor(out=t_lo[:, k, :], in0=main[k][:, :], scalar=tbias[:, k:k + 1],
                                               in1=t_hi[:, k, :].bitcast(F32), op0=ALU.add,
                                               op1=ALU.subtract).then_inc(main_drained, 1)

            def r_of(n, before):
                dve.wait_ge(r_done, before)
                nc.vector.tensor_tensor_reduce(out=unused[:, :], in0=x_rows[:, n, :], in1=u_rows[:, :], scale=1.0,
                                               scalar=r0[:, 0:1], op0=ALU.mult, op1=ALU.add,
                                               accum_out=r_rows[:, n:n + 1]).then_inc(r_done, 1)

            dve.wait_ge(bias_copied, 3)
            for k in range(DC):
                dve.wait_ge(t_hi_done, k + 1)
                t_lo_of(k)
            dve.wait_ge(rows_loaded, 16)
            for n in range(TILES):
                r_of(n, n)
            for c in range(DC):
                dve.wait_ge(wv_hi_done, c + 1)
                lo_of(wv_lo[:, c, :], wv_raw[:, c, :], wv_hi[:, c, :], wv_lo_done)

            def maxima(j, b):
                dve.wait_ge(s_done, j * PB + (b + 1))
                nc.vector.tensor_reduce(negmax[:, b * LT:(b + 1) * LT], score[b][:, :, :], AX_X, ALU.max,
                                        negate=True).then_inc(max_done, 1)
                dve.wait_ge(max_done, j * PB + (b + 1))
                dve.wait_ge(exp_done, j * TILES)
                dve.wait_ge(r_done, j * TILES + TILES)
                for n in range(b * LT, (b + 1) * LT):
                    nc.vector.tensor_scalar(exp_bias[:, n:n + 1], negmax[:, n:n + 1], r_rows[:, n:n + 1],
                                            r_rows[:, n:n + 1], ALU.subtract, ALU.add).then_inc(exp_bias_done, 1)

            def values_lo(j, k):
                dve.wait_ge(v_hi_done, j * TILES + (k + 1))
                lo_of(v_lo[:, k, :], main[k][:, :], v_hi[:, k, :], main_drained)

            def probs_lo(j, b):
                dve.wait_ge(pT_hi_done, j * PB + (b + 1))
                lo_of(pT_lo[:, b, :, :], probT[b][:, :, :], pT_hi[:, b, :, :], pT_lo_done)

            def next_x_lo(j, c):
                dve.wait_ge(x_hi_done, j * DC + (DC + c + 1))
                lo_of(x_lo[:, c, :], x_raw[:, c, :], x_hi[:, c, :], x_lo_done)

            def inverse_sums(j):
                dve.wait_ge(exp_done, j * TILES + TILES)
                nc.vector.reciprocal(inv_sum[:, :], rowsum[:, :]).then_inc(inv_done, 1)

            def outputs(j):
                dve.wait_ge(inv_done, j + 1)
                dve.wait_ge(x_bv_done, j * TILES + TILES)
                dve.wait_ge(stored, j * (16 * PB))
                for k in range(TILES):
                    dve.wait_ge(o_done, j * TILES + (k + 1))
                    nc.vector.scalar_tensor_tensor(out=out_rows[:, k, :], in0=main[k][:, :], scalar=inv_sum[:, k:k + 1],
                                                   in1=x_bv[:, k, :], op0=ALU.mult,
                                                   op1=ALU.add).then_inc(main_drained, 1)

            with dve.Fori(0, PAIRS - 1) as j:
                maxima(j, 0)
                next_x_lo(j, 0)
                maxima(j, 1)
                values_lo(j, 0)
                next_x_lo(j, 1)
                values_lo(j, 1)
                next_x_lo(j, 2)
                probs_lo(j, 0)
                values_lo(j, 2)
                next_x_lo(j, 3)
                probs_lo(j, 1)
                values_lo(j, 3)
                inverse_sums(j)
                dve.wait_ge(rows_loaded, j * 16 + 32)
                for k in range(DC):
                    dve.wait_ge(c_hi_done, j * DC + (DC + k + 1))
                    lo_of(c_lo[:, k, :], c_raw[:, k, :], c_hi[:, k, :], c_lo_done)
                    r_of(k, j * TILES + (TILES + k))
                    dve.wait_ge(t_hi_done, j * DC + (DC + k + 1))
                    t_lo_of(k)
                outputs(j)
            j = PAIRS - 1
            maxima(j, 0)
            maxima(j, 1)
            values_lo(j, 0)
            values_lo(j, 1)
            probs_lo(j, 0)
            values_lo(j, 2)
            probs_lo(j, 1)
            values_lo(j, 3)
            inverse_sums(j)
            outputs(j)

        @block.tensor
        def _(pe):
            def product(dst, a_hi, a_lo, b_hi, b_lo, first, last):
                nc.tensor.matmul(dst, a_hi, b_hi, start=first, stop=False)
                nc.tensor.matmul(dst, a_hi, b_lo, start=False, stop=False)
                return nc.tensor.matmul(dst, a_lo, b_hi, start=False, stop=last)

            def cols(k):
                return slice(k * P, (k + 1) * P)

            for c in range(DC):
                pe.wait_ge(wk_lo_done, c + 1)
                pe.wait_ge(wq_lo_done, c + 1)
                for k in range(DC):
                    mm = product(m_bank[k][:], wq_hi[:, c, cols(k)], wq_lo[:, c, cols(k)],
                                 wk_hi[:, c, :], wk_lo[:, c, :], c == 0, c == DC - 1)
                    if c == DC - 1:
                        mm.then_inc(m_done, 1)

            pe.wait_ge(x_lo_done, DC)
            for c in range(DC):
                pe.wait_ge(m_lo_done, c + 1)
                for k in range(DC):
                    mm = product(main[k][:, :], m_hi[:, c, cols(k)], m_lo[:, c, cols(k)],
                                 x_hi[:, c, :], x_lo[:, c, :], c == 0, c == DC - 1)
                    if c == DC - 1:
                        mm.then_inc(t_done, 1)
                if c == 2:
                    pe.wait_ge(consts_done, 2)
                    pe.wait_ge(parts_done, 1)
                    for k in range(DC):
                        nc.tensor.matmul(score[1][:, 0, k:k + 1], tv_parts[:, cols(k)], ones[:, 0:1],
                                         start=True, stop=True)
                    nc.tensor.matmul(score[1][:, 0, DC:2 * DC], ones[:, :], bqbk[:, :], start=True, stop=True)
                    nc.tensor.matmul(score[0][:], ones[:, :], u_parts[:, :], start=True,
                                     stop=True).then_inc(bias_sums, 1)

            def scores(j):
                pe.wait_ge(c_lo_done, j * DC + DC)
                for b in range(PB):
                    for t in range(LT):
                        q, kk = b * L + t * P, b * L
                        for c in range(DC):
                            mm = product(score[b][:, t, :], t_hi[:, c, q:q + P], t_lo[:, c, q:q + P],
                                         c_hi[:, c, kk:kk + L], c_lo[:, c, kk:kk + L], c == 0, c == DC - 1)
                    mm.then_inc(s_done, 1)

            def values(j, k):
                pe.wait_ge(main_drained, j * 12 + (k + 1))
                for c in range(DC):
                    mm = product(main[k][:, :], c_hi[:, c, cols(k)], c_lo[:, c, cols(k)],
                                 wv_hi[:, c, :], wv_lo[:, c, :], c == 0, c == DC - 1)
                mm.then_inc(v_done, 1)

            def transposes(j, b):
                pe.wait_ge(exp_done, j * TILES + (b * LT + LT))
                for t in range(LT):
                    for kt in range(LT):
                        mm = nc.tensor.transpose(probT[b][:, kt, cols(t)], probs[:, b, t, cols(kt)], ident[:, :])
                mm.then_inc(pT_done, 1)

            def scores_and_values(j):
                scores(j)
                values(j, 0)
                values(j, 1)
                transposes(j, 0)
                values(j, 2)
                transposes(j, 1)
                values(j, 3)

            def outputs(j, drained_before):
                for b in range(PB):
                    pe.wait_ge(pT_lo_done, j * PB + (b + 1))
                    for t in range(LT):
                        k = b * LT + t
                        pe.wait_ge(main_drained, drained_before(j, k))
                        for kt in range(LT):
                            v = b * LT + kt
                            mm = product(main[k][:, :], pT_hi[:, b, kt, cols(t)], pT_lo[:, b, kt, cols(t)],
                                         v_hi[:, v, :], v_lo[:, v, :], kt == 0, kt == LT - 1)
                        mm.then_inc(o_done, 1)

            pe.wait_ge(main_drained, DC)
            pe.wait_ge(bias_copied, 3)
            pe.wait_ge(wv_lo_done, DC)
            with pe.Fori(0, PAIRS - 1) as j:
                scores_and_values(j)
                pe.wait_ge(x_lo_done, j * DC + 2 * DC)
                for k in range(DC):
                    pe.wait_ge(main_drained, drained_v(j, k))
                    for c in range(DC):
                        mm = product(main[k][:, :], m_hi[:, c, cols(k)], m_lo[:, c, cols(k)],
                                     x_hi[:, c, :], x_lo[:, c, :], c == 0, c == DC - 1)
                    mm.then_inc(t_done, 1)
                outputs(j, drained_t_next)
            scores_and_values(PAIRS - 1)
            pe.wait_ge(main_drained, drained_v(PAIRS - 1, TILES - 1))
            outputs(PAIRS - 1, drained_v)


def kernel(x, ctx_1024, L0_xattn_Wq, L0_xattn_bq, L0_xattn_Wk, L0_xattn_bk, L0_xattn_Wv, L0_xattn_bv):
    import numpy as np
    import concourse.bacc as bacc
    from concourse.bass_utils import run_bass_kernel_spmd

    B, L, D = x.shape
    pairs, chunks, tiles = B // PB, D // P, L // P
    x, c = np.asarray(x), np.asarray(ctx_1024)
    xT = x.reshape(pairs, PB, P, tiles, chunks, P).transpose(0, 5, 4, 1, 3, 2).reshape(pairs, P, chunks, PB * L)
    cT = c.reshape(pairs, PB, L, chunks, P).transpose(0, 4, 3, 1, 2).reshape(pairs, P, chunks, PB * L)
    arrays = {
        "x": x,
        "xT": xT,
        "cT": cT,
        "WqT": np.asarray(L0_xattn_Wq).T.reshape(chunks, P, D),
        "WkT": np.asarray(L0_xattn_Wk).T.reshape(chunks, P, D),
        "Wv": np.asarray(L0_xattn_Wv),
        "bq": np.asarray(L0_xattn_bq).reshape(chunks, P).T,
        "bk": np.asarray(L0_xattn_bk).reshape(chunks, P).T,
        "bv": np.asarray(L0_xattn_bv).reshape(1, D),
    }
    arrays = {f"in_{name}_dram": np.ascontiguousarray(a) for name, a in arrays.items()}
    nc = bacc.Bacc("TRN2", target_bir_lowering=False, num_devices=1)
    args = [nc.dram_tensor(name, a.shape, mybir.dt.from_np(a.dtype), kind="ExternalInput").ap()
            for name, a in arrays.items()]
    out = nc.dram_tensor("out_dram", (B, L, D), F32, kind="ExternalOutput").ap()
    xattn_program(nc, *args, out)
    r = run_bass_kernel_spmd(nc, [arrays], core_ids=[0])
    return r.results[0]["out_dram"]
```

```python
from contextlib import ExitStack

import concourse.bass as bass
from concourse import mybir

F32 = mybir.dt.float32
F32R = mybir.dt.float32r
ALU = mybir.AluOpType
ACT = mybir.ActivationFunctionType
AX_X = mybir.AxisListType.X

P = 128
PB = 2


def xattn_program(nc, x, xT, cT, WqT, WkT, Wv, bq, bk, bv, out):
    B, L, D = x.shape
    PAIRS = B // PB
    DC = D // P
    LT = L // P
    COLS = PB * L
    TILES = PB * LT
    assert COLS == 512 and D == 512 and DC == TILES == 4 and LT == 2

    with ExitStack() as ctx:
        def sb(name, shape, dt=F32):
            return ctx.enter_context(nc.sbuf_tensor(name, shape, dt))

        def sem(name):
            return ctx.enter_context(nc.semaphore(name))

        wk_raw = sb("wk_raw", [P, DC, D])
        wk_hi, wk_lo = sb("wk_hi", [P, DC, D], F32R), sb("wk_lo", [P, DC, D], F32R)
        wv_hi, wv_lo = sb("wv_hi", [P, DC, D], F32R), sb("wv_lo", [P, DC, D], F32R)
        m_hi, m_lo = sb("m_hi", [P, DC, D], F32R), sb("m_lo", [P, DC, D], F32R)
        x_raw = sb("x_raw", [P, DC, COLS])
        x_hi, x_lo = sb("x_hi", [P, DC, COLS], F32R), sb("x_lo", [P, DC, COLS], F32R)
        c_raw = sb("c_raw", [P, DC, COLS])
        c_hi, c_lo = sb("c_hi", [P, DC, COLS], F32R), sb("c_lo", [P, DC, COLS], F32R)
        t_hi, t_lo = sb("t_hi", [P, DC, COLS], F32R), sb("t_lo", [P, DC, COLS], F32R)
        v_hi, v_lo = sb("v_hi", [P, TILES, D], F32R), sb("v_lo", [P, TILES, D], F32R)
        probs = sb("probs", [P, PB, LT, L])
        pT_hi, pT_lo = sb("pT_hi", [P, PB, LT, L], F32R), sb("pT_lo", [P, PB, LT, L], F32R)
        x_rows = sb("x_rows", [P, TILES, D])
        x_bv = sb("x_bv", [P, TILES, D])
        out_rows = sb("out_rows", [P, TILES, D])
        bv_rows = sb("bv_rows", [P, D])
        u_rows = sb("u_rows", [P, D])
        u_parts = sb("u_parts", [P, D])
        tv_parts = sb("tv_parts", [P, D])
        scaled = sb("scaled", [P, 2, D])
        unused = sb("unused", [P, D])
        bq_col, bk_col = sb("bq_col", [P, DC]), sb("bk_col", [P, DC])
        bqbk = sb("bqbk", [P, DC])
        tbias = sb("tbias", [P, DC])
        r0 = sb("r0", [P, 1])
        r_rows = sb("r_rows", [P, TILES])
        negmax = sb("negmax", [P, TILES])
        exp_bias = sb("exp_bias", [P, TILES])
        rowsum = sb("rowsum", [P, TILES])
        inv_sum = sb("inv_sum", [P, TILES])
        ident = sb("ident", [P, P])
        ones = sb("ones", [P, P])
        wq_raw, wv_raw = x_bv, out_rows
        wq_hi, wq_lo = v_hi, v_lo

        main = [ctx.enter_context(nc.psum_tensor(f"main{k}", [P, 512], F32)) for k in range(4)]
        score = [ctx.enter_context(nc.psum_tensor(f"score{b}", [P, LT, L], F32)) for b in range(PB)]
        probT = [ctx.enter_context(nc.psum_tensor(f"probT{b}", [P, LT, L], F32)) for b in range(PB)]
        m_bank = [score[0], score[1], probT[0], probT[1]]

        wk_loaded = [sem(f"wk_loaded{c}") for c in range(DC)]
        wq_first_loaded = sem("wq_first_loaded")
        wq_loaded = [sem(f"wq_loaded{c}") for c in range(DC)]
        bqk_loaded, bv_loaded = sem("bqk_loaded"), sem("bv_loaded")
        x_loaded, c_loaded, rows_loaded = sem("x_loaded"), sem("c_loaded"), sem("rows_loaded")
        out_rows_moved = sem("out_rows_moved")
        wk_hi_done, wq_hi_done, wv_hi_done, m_hi_done = sem("wk_hi_done"), sem("wq_hi_done"), sem("wv_hi_done"), sem("m_hi_done")
        wk_lo_done, wq_lo_done, wv_lo_done, m_lo_done = sem("wk_lo_done"), sem("wq_lo_done"), sem("wv_lo_done"), sem("m_lo_done")
        x_hi_done, c_hi_done, t_hi_done, v_hi_done, pT_hi_done = (
            sem("x_hi_done"), sem("c_hi_done"), sem("t_hi_done"), sem("v_hi_done"), sem("pT_hi_done"))
        x_lo_done, c_lo_done, pT_lo_done = sem("x_lo_done"), sem("c_lo_done"), sem("pT_lo_done")
        main_drained = sem("main_drained")
        m_done, t_done, v_done, s_done, pT_done, o_done = (
            sem("m_done"), sem("t_done"), sem("v_done"), sem("s_done"), sem("pT_done"), sem("o_done"))
        tv_parts_done, tv_sums, u_sums, bias_copied = sem("tv_parts_done"), sem("tv_sums"), sem("u_sums"), sem("bias_copied")
        max_done, exp_bias_done, exp_done, inv_done, r_done = (
            sem("max_done"), sem("exp_bias_done"), sem("exp_done"), sem("inv_done"), sem("r_done"))
        ident_zero, consts_done, pool_step, parts_done, x_bv_done = (
            sem("ident_zero"), sem("consts_done"), sem("pool_step"), sem("parts_done"), sem("x_bv_done"))

        def drained_v(j, k):
            return j * 12 + (TILES + k + 1)

        def drained_t_next(j, k):
            return j * 12 + (2 * TILES + k + 1)

        def drained_o(j, k):
            return j * 12 + (3 * TILES + k + 1)

        def steps_of(engine, n):
            return nc.Fori(0, n, engines=[engine.engine], hint_back_edge=True)

        def rows_of(dram, j):
            return dram[bass.ds(j * PB, PB)].rearrange("b (p t) d -> p b (t d)", t=LT)

        def sb_rows(tensor):
            return tensor[:, :, :].rearrange("p (b t) d -> p b (t d)", b=PB)

        block = ctx.enter_context(nc.Block())

        @block.sync
        def _(sp):
            for c in range(DC):
                sp.dma_start(wk_raw[:, c, :], WkT[c]).then_inc(wk_loaded[c], 16)
                if c == 0:
                    sp.dma_start(wq_raw[:, 0, 0:P], WqT[0][:, 0:P]).then_inc(wq_first_loaded, 16)
                    sp.dma_start(wq_raw[:, 0, P:D], WqT[0][:, P:D]).then_inc(wq_loaded[0], 16)
                else:
                    sp.dma_start(wq_raw[:, c, :], WqT[c]).then_inc(wq_loaded[c], 16)
                if c == 1:
                    sp.dma_start(bq_col[:, :], bq).then_inc(bqk_loaded, 16)
                    sp.dma_start(bk_col[:, :], bk).then_inc(bqk_loaded, 16)
            sp.dma_start(x_raw[:, :, :], xT[0]).then_inc(x_loaded, 16)
            sp.dma_start(c_raw[:, :, :], cT[0]).then_inc(c_loaded, 16)
            sp.dma_start(wv_raw[:, :, :], Wv.rearrange("(c p) e -> p c e", p=P)).then_inc(out_rows_moved, 16)
            sp.dma_start(sb_rows(x_rows), rows_of(x, 0)).then_inc(rows_loaded, 16)
            sp.dma_start(bv_rows[:, :], bv.to_broadcast([P, D])).then_inc(bv_loaded, 16)
            sp.wait_ge(x_lo_done, DC)
            sp.dma_start(x_raw[:, :, :], xT[1]).then_inc(x_loaded, 16)
            sp.wait_ge(c_lo_done, DC)
            sp.dma_start(c_raw[:, :, :], cT[1]).then_inc(c_loaded, 16)
            sp.wait_ge(x_bv_done, TILES)
            sp.wait_ge(r_done, TILES)
            sp.dma_start(sb_rows(x_rows), rows_of(x, 1)).then_inc(rows_loaded, 16)

            def store(b, j, drained):
                sp.wait_ge(main_drained, drained)
                sp.dma_start(rows_of(out, j)[:, b], sb_rows(out_rows)[:, b]).then_inc(out_rows_moved, 16)

            with steps_of(sp, PAIRS - 2) as j:
                sp.wait_ge(x_lo_done, j * DC + 2 * DC)
                sp.dma_start(x_raw[:, :, :], xT[bass.ds(j + 2, 1)].rearrange("a p c q -> p (a c) q")).then_inc(x_loaded, 16)
                sp.wait_ge(c_lo_done, j * DC + 2 * DC)
                sp.dma_start(c_raw[:, :, :], cT[bass.ds(j + 2, 1)].rearrange("a p c q -> p (a c) q")).then_inc(c_loaded, 16)
                for b in range(PB):
                    store(b, j, drained_o(j, b * LT + LT - 1))
                sp.wait_ge(x_bv_done, j * TILES + 2 * TILES)
                sp.wait_ge(r_done, j * TILES + 2 * TILES)
                sp.dma_start(sb_rows(x_rows), rows_of(x, j + 2)).then_inc(rows_loaded, 16)
            for b in range(PB):
                store(b, PAIRS - 2, drained_o(PAIRS - 2, b * LT + LT - 1))
            for k in range(TILES):
                sp.wait_ge(main_drained, drained_t_next(PAIRS - 1, k))
                b, t = k // LT, k % LT
                sp.dma_start(rows_of(out, PAIRS - 1)[:, b, t * D:(t + 1) * D], out_rows[:, k, :]).then_inc(out_rows_moved, 16)
            sp.wait_ge(out_rows_moved, 16 + 16 * (B - PB) + 16 * TILES)

        @block.gpsimd
        def _(pool):
            pool.memset(ident[:, :], 0.0).then_inc(ident_zero, 1)
            pool.memset(ones[:, :], 1.0).then_inc(consts_done, 1)
            pool.wait_ge(ident_zero, 1)
            pool.affine_select(out=ident[:, :], in_=ident[:, :], compare_op=ALU.not_equal, fill=1.0, base=0,
                               pattern=[[-1, P]], channel_multiplier=1).then_inc(consts_done, 1)

            pool.wait_ge(bqk_loaded, 32)
            steps = [0]

            def step(ins):
                steps[0] += 1
                ins.then_inc(pool_step, 1)

            pool.wait_ge(wq_first_loaded, 16)
            for c in range(DC):
                pool.wait_ge(wq_loaded[c], 16)
                if c == 0:
                    step(pool.tensor_scalar(u_parts[:, :], wq_raw[:, c, :], bk_col[:, c:c + 1], None, ALU.mult))
                else:
                    step(pool.tensor_scalar(scaled[:, c % 2, :], wq_raw[:, c, :], bk_col[:, c:c + 1], None, ALU.mult))
                    pool.wait_ge(pool_step, steps[0])
                    step(pool.tensor_tensor(u_parts[:, :], u_parts[:, :], scaled[:, c % 2, :], ALU.add))
            pool.wait_ge(pool_step, steps[0])
            pool.tensor_tensor(bqbk[:, :], bq_col[:, :], bk_col[:, :], ALU.mult).then_inc(parts_done, 1)

            def residual(j):
                pool.wait_ge(rows_loaded, j * 16 + 16)
                for t in range(TILES):
                    pool.tensor_tensor(x_bv[:, t, :], x_rows[:, t, :], bv_rows[:, :], ALU.add).then_inc(x_bv_done, 1)

            pool.wait_ge(bv_loaded, 16)
            pool.wait_ge(wq_lo_done, DC + 1)
            residual(0)
            with steps_of(pool, PAIRS - 1) as j:
                pool.wait_ge(main_drained, drained_o(j, TILES - 1))
                residual(j + 1)

        @block.scalar
        def _(act):
            def hi_of(hi, raw, done):
                nc.scalar.copy(hi, raw).then_inc(done, 1)

            for c in range(DC):
                act.wait_ge(wk_loaded[c], 16)
                hi_of(wk_hi[:, c, :], wk_raw[:, c, :], wk_hi_done)
                first = P if c == 0 else 0
                if c == 0:
                    act.wait_ge(wq_first_loaded, 16)
                    hi_of(wq_hi[:, 0, 0:P], wq_raw[:, 0, 0:P], wq_hi_done)
                act.wait_ge(wq_loaded[c], 16)
                hi_of(wq_hi[:, c, first:D], wq_raw[:, c, first:D], wq_hi_done)
            act.wait_ge(x_loaded, 16)
            for c in range(DC):
                hi_of(x_hi[:, c, :], x_raw[:, c, :], x_hi_done)
            for k in range(DC):
                act.wait_ge(m_done, k + 1)
                hi_of(m_hi[:, k, :], m_bank[k][:], m_hi_done)
            act.wait_ge(c_loaded, 16)
            for c in range(DC):
                hi_of(c_hi[:, c, :], c_raw[:, c, :], c_hi_done)

            def t_hi_of(k):
                nc.scalar.activation(t_hi[:, k, :], main[k][:, :], ACT.Identity,
                                     bias=tbias[:, k:k + 1]).then_inc(t_hi_done, 1)

            act.wait_ge(out_rows_moved, 16)
            for c in range(DC):
                hi_of(wv_hi[:, c, :], wv_raw[:, c, :], wv_hi_done)
            act.wait_ge(bias_copied, 1)
            for k in range(DC):
                act.wait_ge(t_done, k + 1)
                t_hi_of(k)

            def exponentials(j, b):
                act.wait_ge(exp_bias_done, j * TILES + (b * LT + LT))
                for t in range(LT):
                    n = b * LT + t
                    nc.scalar.activation(probs[:, b, t, :], score[b][:, t, :], ACT.Exp, bias=exp_bias[:, n:n + 1],
                                         accum_out=rowsum[:, n:n + 1]).then_inc(exp_done, 1)

            def values_hi(j, k):
                act.wait_ge(v_done, j * TILES + (k + 1))
                hi_of(v_hi[:, k, :], main[k][:, :], v_hi_done)

            def probs_hi(j, b):
                act.wait_ge(pT_done, j * PB + (b + 1))
                hi_of(pT_hi[:, b, :, :], probT[b][:, :, :], pT_hi_done)

            def softmax_and_values(j):
                exponentials(j, 0)
                exponentials(j, 1)
                values_hi(j, 0)
                values_hi(j, 1)
                probs_hi(j, 0)
                values_hi(j, 2)
                probs_hi(j, 1)
                values_hi(j, 3)

            with steps_of(act, PAIRS - 1) as j:
                act.wait_ge(x_loaded, j * 16 + 32)
                act.wait_ge(t_done, j * DC + DC)
                for c in range(DC):
                    hi_of(x_hi[:, c, :], x_raw[:, c, :], x_hi_done)
                softmax_and_values(j)
                act.wait_ge(c_loaded, j * 16 + 32)
                for k in range(DC):
                    hi_of(c_hi[:, k, :], c_raw[:, k, :], c_hi_done)
                    act.wait_ge(t_done, j * DC + (DC + k + 1))
                    t_hi_of(k)
            softmax_and_values(PAIRS - 1)

        @block.vector
        def _(dve):
            def lo_of(lo, raw, hi, done):
                nc.vector.tensor_tensor(lo, raw, hi.bitcast(F32), ALU.subtract).then_inc(done, 1)

            for c in range(DC):
                dve.wait_ge(wk_hi_done, c + 1)
                lo_of(wk_lo[:, c, :], wk_raw[:, c, :], wk_hi[:, c, :], wk_lo_done)
                first = P if c == 0 else 0
                if c == 0:
                    dve.wait_ge(wq_hi_done, 1)
                    lo_of(wq_lo[:, 0, 0:P], wq_raw[:, 0, 0:P], wq_hi[:, 0, 0:P], wq_lo_done)
                dve.wait_ge(wq_hi_done, c + 2)
                lo_of(wq_lo[:, c, first:D], wq_raw[:, c, first:D], wq_hi[:, c, first:D], wq_lo_done)
            for c in range(DC):
                dve.wait_ge(x_hi_done, c + 1)
                lo_of(x_lo[:, c, :], x_raw[:, c, :], x_hi[:, c, :], x_lo_done)
            dve.wait_ge(bqk_loaded, 32)
            nc.vector.tensor_scalar(tv_parts[:, :], wk_raw[:, 0, :], bq_col[:, 0:1], None, ALU.mult).then_inc(tv_parts_done, 1)
            for c in range(1, DC):
                dve.wait_ge(tv_parts_done, c)
                nc.vector.scalar_tensor_tensor(out=tv_parts[:, :], in0=wk_raw[:, c, :], scalar=bq_col[:, c:c + 1],
                                               in1=tv_parts[:, :], op0=ALU.mult, op1=ALU.add).then_inc(tv_parts_done, 1)
            for k in range(DC):
                dve.wait_ge(m_hi_done, k + 1)
                lo_of(m_lo[:, k, :], m_bank[k][:], m_hi[:, k, :], m_lo_done)
            for c in range(DC):
                dve.wait_ge(c_hi_done, c + 1)
                lo_of(c_lo[:, c, :], c_raw[:, c, :], c_hi[:, c, :], c_lo_done)
            dve.wait_ge(tv_sums, 1)
            nc.vector.tensor_copy(tbias[:, :], score[1][:, 0, 0:DC]).then_inc(bias_copied, 1)
            for c in range(DC):
                dve.wait_ge(wv_hi_done, c + 1)
                lo_of(wv_lo[:, c, :], wv_raw[:, c, :], wv_hi[:, c, :], wv_lo_done)

            def t_lo_of(k):
                nc.vector.scalar_tensor_tensor(out=t_lo[:, k, :], in0=main[k][:, :], scalar=tbias[:, k:k + 1],
                                               in1=t_hi[:, k, :].bitcast(F32), op0=ALU.add,
                                               op1=ALU.subtract).then_inc(main_drained, 1)

            def r_of(n, before):
                dve.wait_ge(r_done, before)
                nc.vector.tensor_tensor_reduce(out=unused[:, :], in0=x_rows[:, n, :], in1=u_rows[:, :], scale=1.0,
                                               scalar=r0[:, 0:1], op0=ALU.mult, op1=ALU.add,
                                               accum_out=r_rows[:, n:n + 1]).then_inc(r_done, 1)

            for k in range(DC):
                dve.wait_ge(t_hi_done, k + 1)
                t_lo_of(k)
            dve.wait_ge(u_sums, 1)
            nc.vector.reduce_sum(r0[:, :], probT[0][:, 0, 0:DC], AX_X).then_inc(bias_copied, 1)
            nc.vector.tensor_copy(u_rows[:, :].rearrange("p (a b) -> p a b", a=LT), probT[1][:, :, :]).then_inc(bias_copied, 1)
            dve.wait_ge(rows_loaded, 16)
            dve.wait_ge(bias_copied, 3)
            for n in range(TILES):
                r_of(n, n)

            def maxima(j, b):
                dve.wait_ge(s_done, j * PB + (b + 1))
                nc.vector.tensor_reduce(negmax[:, b * LT:(b + 1) * LT], score[b][:, :, :], AX_X, ALU.max,
                                        negate=True).then_inc(max_done, 1)
                dve.wait_ge(max_done, j * PB + (b + 1))
                dve.wait_ge(r_done, j * TILES + TILES)
                for n in range(b * LT, (b + 1) * LT):
                    nc.vector.tensor_scalar(exp_bias[:, n:n + 1], negmax[:, n:n + 1], r_rows[:, n:n + 1],
                                            r_rows[:, n:n + 1], ALU.subtract, ALU.add).then_inc(exp_bias_done, 1)

            def values_lo(j, k):
                dve.wait_ge(v_hi_done, j * TILES + (k + 1))
                lo_of(v_lo[:, k, :], main[k][:, :], v_hi[:, k, :], main_drained)

            def probs_lo(j, b):
                dve.wait_ge(pT_hi_done, j * PB + (b + 1))
                lo_of(pT_lo[:, b, :, :], probT[b][:, :, :], pT_hi[:, b, :, :], pT_lo_done)

            def next_x_lo(j, c):
                dve.wait_ge(x_hi_done, j * DC + (DC + c + 1))
                lo_of(x_lo[:, c, :], x_raw[:, c, :], x_hi[:, c, :], x_lo_done)

            def inverse_sums(j):
                dve.wait_ge(exp_done, j * TILES + TILES)
                nc.vector.reciprocal(inv_sum[:, :], rowsum[:, :]).then_inc(inv_done, 1)

            def outputs(j):
                dve.wait_ge(inv_done, j + 1)
                dve.wait_ge(x_bv_done, j * TILES + TILES)
                dve.wait_ge(out_rows_moved, j * (16 * PB) + 16)
                for k in range(TILES):
                    dve.wait_ge(o_done, j * TILES + (k + 1))
                    nc.vector.scalar_tensor_tensor(out=out_rows[:, k, :], in0=main[k][:, :], scalar=inv_sum[:, k:k + 1],
                                                   in1=x_bv[:, k, :], op0=ALU.mult,
                                                   op1=ALU.add).then_inc(main_drained, 1)

            with steps_of(dve, PAIRS - 1) as j:
                maxima(j, 0)
                next_x_lo(j, 0)
                maxima(j, 1)
                values_lo(j, 0)
                next_x_lo(j, 1)
                values_lo(j, 1)
                next_x_lo(j, 2)
                probs_lo(j, 0)
                values_lo(j, 2)
                next_x_lo(j, 3)
                probs_lo(j, 1)
                values_lo(j, 3)
                inverse_sums(j)
                dve.wait_ge(rows_loaded, j * 16 + 32)
                for k in range(DC):
                    dve.wait_ge(c_hi_done, j * DC + (DC + k + 1))
                    lo_of(c_lo[:, k, :], c_raw[:, k, :], c_hi[:, k, :], c_lo_done)
                    r_of(k, j * TILES + (TILES + k))
                    dve.wait_ge(t_hi_done, j * DC + (DC + k + 1))
                    t_lo_of(k)
                outputs(j)
            j = PAIRS - 1
            maxima(j, 0)
            maxima(j, 1)
            values_lo(j, 0)
            values_lo(j, 1)
            probs_lo(j, 0)
            values_lo(j, 2)
            probs_lo(j, 1)
            values_lo(j, 3)
            inverse_sums(j)
            outputs(j)

        @block.tensor
        def _(pe):
            def product(dst, a_hi, a_lo, b_hi, b_lo, first, last):
                nc.tensor.matmul(dst, a_hi, b_hi, start=first, stop=False)
                nc.tensor.matmul(dst, a_hi, b_lo, start=False, stop=False)
                return nc.tensor.matmul(dst, a_lo, b_hi, start=False, stop=last)

            def cols(k):
                return slice(k * P, (k + 1) * P)

            for c in range(DC):
                pe.wait_ge(wk_lo_done, c + 1)
                for k in range(DC):
                    if c == 0 and k < 2:
                        pe.wait_ge(wq_lo_done, k + 1)
                    elif k == 0:
                        pe.wait_ge(wq_lo_done, c + 2)
                    mm = product(m_bank[k][:], wq_hi[:, c, cols(k)], wq_lo[:, c, cols(k)],
                                 wk_hi[:, c, :], wk_lo[:, c, :], c == 0, c == DC - 1)
                    if c == DC - 1:
                        mm.then_inc(m_done, 1)

            pe.wait_ge(x_lo_done, DC)
            for c in range(DC):
                pe.wait_ge(m_lo_done, c + 1)
                for k in range(DC):
                    mm = product(main[k][:, :], m_hi[:, c, cols(k)], m_lo[:, c, cols(k)],
                                 x_hi[:, c, :], x_lo[:, c, :], c == 0, c == DC - 1)
                    if c == DC - 1:
                        mm.then_inc(t_done, 1)
                if c == 1:
                    pe.wait_ge(consts_done, 2)
                    pe.wait_ge(tv_parts_done, DC)
                    for k in range(DC):
                        mm = nc.tensor.matmul(score[1][:, 0, k:k + 1], tv_parts[:, cols(k)], ones[:, 0:1],
                                              start=True, stop=True)
                    mm.then_inc(tv_sums, 1)
            pe.wait_ge(parts_done, 1)
            nc.tensor.matmul(probT[0][:, 0, 0:DC], ones[:, :], bqbk[:, :], start=True, stop=True)
            nc.tensor.matmul(probT[1][:], ones[:, :], u_parts[:, :], start=True, stop=True).then_inc(u_sums, 1)

            def scores(j, first=False):
                pe.wait_ge(c_lo_done, j * DC + DC)
                for b in range(PB):
                    for t in range(LT):
                        q, kk = b * L + t * P, b * L
                        for c in range(DC):
                            if first and (b, t) == (0, 0):
                                pe.wait_ge(main_drained, c + 1)
                            mm = product(score[b][:, t, :], t_hi[:, c, q:q + P], t_lo[:, c, q:q + P],
                                         c_hi[:, c, kk:kk + L], c_lo[:, c, kk:kk + L], c == 0, c == DC - 1)
                    mm.then_inc(s_done, 1)

            def values(j, k):
                pe.wait_ge(main_drained, j * 12 + (k + 1))
                for c in range(DC):
                    mm = product(main[k][:, :], c_hi[:, c, cols(k)], c_lo[:, c, cols(k)],
                                 wv_hi[:, c, :], wv_lo[:, c, :], c == 0, c == DC - 1)
                mm.then_inc(v_done, 1)

            def transposes(j, b):
                pe.wait_ge(exp_done, j * TILES + (b * LT + LT))
                for t in range(LT):
                    for kt in range(LT):
                        mm = nc.tensor.transpose(probT[b][:, kt, cols(t)], probs[:, b, t, cols(kt)], ident[:, :])
                mm.then_inc(pT_done, 1)

            def values_and_transposes(j):
                values(j, 0)
                values(j, 1)
                transposes(j, 0)
                values(j, 2)
                transposes(j, 1)
                values(j, 3)

            def outputs(j, drained_before):
                for b in range(PB):
                    pe.wait_ge(pT_lo_done, j * PB + (b + 1))
                    pe.wait_ge(main_drained, drained_v(j, b * LT + LT - 1))
                    for t in range(LT):
                        k = b * LT + t
                        pe.wait_ge(main_drained, drained_before(j, k))
                        for kt in range(LT):
                            v = b * LT + kt
                            mm = product(main[k][:, :], pT_hi[:, b, kt, cols(t)], pT_lo[:, b, kt, cols(t)],
                                         v_hi[:, v, :], v_lo[:, v, :], kt == 0, kt == LT - 1)
                        mm.then_inc(o_done, 1)

            pe.wait_ge(bias_copied, 1)
            scores(0, first=True)
            pe.wait_ge(wv_lo_done, DC)
            with steps_of(pe, PAIRS - 1) as j:
                values_and_transposes(j)
                pe.wait_ge(x_lo_done, j * DC + 2 * DC)
                for k in range(DC):
                    pe.wait_ge(main_drained, drained_v(j, k))
                    for c in range(DC):
                        mm = product(main[k][:, :], m_hi[:, c, cols(k)], m_lo[:, c, cols(k)],
                                     x_hi[:, c, :], x_lo[:, c, :], c == 0, c == DC - 1)
                    mm.then_inc(t_done, 1)
                outputs(j, drained_t_next)
                scores(j + 1)
            values_and_transposes(PAIRS - 1)
            outputs(PAIRS - 1, drained_v)


def kernel(x, ctx_1024, L0_xattn_Wq, L0_xattn_bq, L0_xattn_Wk, L0_xattn_bk, L0_xattn_Wv, L0_xattn_bv):
    import numpy as np
    import concourse.bacc as bacc
    from concourse.bass_utils import run_bass_kernel_spmd

    B, L, D = x.shape
    pairs, chunks, tiles = B // PB, D // P, L // P
    x, c = np.asarray(x), np.asarray(ctx_1024)
    xT = x.reshape(pairs, PB, P, tiles, chunks, P).transpose(0, 5, 4, 1, 3, 2).reshape(pairs, P, chunks, PB * L)
    cT = c.reshape(pairs, PB, L, chunks, P).transpose(0, 4, 3, 1, 2).reshape(pairs, P, chunks, PB * L)
    arrays = {
        "x": x,
        "xT": xT,
        "cT": cT,
        "WqT": np.asarray(L0_xattn_Wq).T.reshape(chunks, P, D),
        "WkT": np.asarray(L0_xattn_Wk).T.reshape(chunks, P, D),
        "Wv": np.asarray(L0_xattn_Wv),
        "bq": np.asarray(L0_xattn_bq).reshape(chunks, P).T,
        "bk": np.asarray(L0_xattn_bk).reshape(chunks, P).T,
        "bv": np.asarray(L0_xattn_bv).reshape(1, D),
    }
    arrays = {f"in_{name}_dram": np.ascontiguousarray(a) for name, a in arrays.items()}
    nc = bacc.Bacc("TRN2", target_bir_lowering=False, num_devices=1)
    args = [nc.dram_tensor(name, a.shape, mybir.dt.from_np(a.dtype), kind="ExternalInput").ap()
            for name, a in arrays.items()]
    out = nc.dram_tensor("out_dram", (B, L, D), F32, kind="ExternalOutput").ap()
    xattn_program(nc, *args, out)
    r = run_bass_kernel_spmd(nc, [arrays], core_ids=[0])
    return r.results[0]["out_dram"]
```
